# Optimizing a Trainium2 kernel written in Bass

```python
import numpy as np
import jax
import jax.numpy as jnp

def _softmax(x, axis=-1):
    return jax.nn.softmax(x, axis=axis)
def _gelu(x):
    return jax.nn.gelu(x, approximate=True)
def _silu(x):
    return jax.nn.silu(x)
def _sigmoid(x):
    return jax.nn.sigmoid(x)
def _layernorm(x, axis=-1, eps=1e-5):
    m = jnp.mean(x, axis=axis, keepdims=True)
    v = jnp.var(x, axis=axis, keepdims=True)
    return (x - m) / jnp.sqrt(v + eps)
def _scatter_add(tgt, idx, src, axis=0):
    return tgt.at[idx].add(src)
def _segment_sum(src, seg, n):
    return jax.ops.segment_sum(src, seg, n)

kernel_name = 'mk_conv_seq_d1_conv_nchw256_c1fbc5'

def setup_inputs(seed: int = 0):
    np.random.seed(seed)
    _w = jnp.asarray
    def _rec_inputs():
        import jax
        import jax.numpy as jnp
        _gk = jax.random.key(seed)
        x = -7.109e-05 + 0.9999 * jax.random.normal(jax.random.fold_in(_gk, 1), (16, 256, 128, 128), jnp.float32)
        return x
    x = _rec_inputs()
    def _L0_conv_setup():
        import jax, jax.numpy as jnp
        import numpy as np
        import math
        B, C, H, W = (16, 256, 128, 128)
        IC = 32
        key = jax.random.key(seed)
        ks = jax.random.split(key, 7)
        s_in = 1.0 / math.sqrt(C)
        s_out = 1.0 / math.sqrt(IC)
        return {'x': jax.random.normal(ks[0], (B, C, H, W), dtype=jnp.float32), 'g_w': jax.random.normal(ks[1], (IC, C), dtype=jnp.float32) * s_in, 'g_b': jax.random.normal(ks[2], (IC,), dtype=jnp.float32) * s_in, 'theta_w': jax.random.normal(ks[3], (IC, C), dtype=jnp.float32) * s_in, 'theta_b': jax.random.normal(ks[4], (IC,), dtype=jnp.float32) * s_in, 'w_w': jax.random.normal(ks[5], (C, IC), dtype=jnp.float32) * s_out, 'w_b': jax.random.normal(ks[6], (C,), dtype=jnp.float32) * s_out}
    _L0_conv_all = _L0_conv_setup()
    _L0_conv_in = {k: v for k, v in _L0_conv_all.items() if k in ('g_w', 'g_b', 'theta_w', 'theta_b', 'w_w', 'w_b', )}
    del _L0_conv_all

    return {
        "x": x,
        "L0_conv_g_w": _L0_conv_in["g_w"],
        "L0_conv_g_b": _L0_conv_in["g_b"],
        "L0_conv_theta_w": _L0_conv_in["theta_w"],
        "L0_conv_theta_b": _L0_conv_in["theta_b"],
        "L0_conv_w_w": _L0_conv_in["w_w"],
        "L0_conv_w_b": _L0_conv_in["w_b"],
    }

def reference(x, L0_conv_g_w, L0_conv_g_b, L0_conv_theta_w, L0_conv_theta_b, L0_conv_w_w, L0_conv_w_b):
    import jax
    import jax.numpy as jnp
    def _L0_conv_ref(x, g_w, g_b, theta_w, theta_b, w_w, w_b):
        import jax, jax.numpy as jnp
        import numpy as np
        import math
        B, C, H, W = (16, 256, 128, 128)
        IC = 32
        b, c, h, w = x.shape
        m = h * w
        ic = g_w.shape[0]
        xf = x.reshape(b, c, m)
        g_x = jnp.einsum('ic,bcm->bim', g_w, xf) + g_b[None, :, None]
        t = jnp.einsum('ic,bcm->bim', theta_w, xf) + theta_b[None, :, None]
        mu = jnp.mean(t, axis=-1)
        sigma = jnp.einsum('bim,bjm->bij', t, t) / m - mu[:, :, None] * mu[:, None, :]
        sigma = sigma / math.sqrt(ic)
        attn = jax.nn.softmax(sigma, axis=-1)
        y = jnp.einsum('bij,bjm->bim', attn, g_x)
        w_y = jnp.einsum('ci,bim->bcm', w_w, y) + w_b[None, :, None]
        return (w_y + xf).reshape(b, c, h, w)

    def _gn(v, G=32, eps=1e-5):
        B_, C_, H_, W_ = v.shape
        g = v.reshape(B_, G, C_ // G, H_, W_)
        m = jnp.mean(g, axis=(2, 3, 4), keepdims=True)
        s = jnp.var(g, axis=(2, 3, 4), keepdims=True)
        return ((g - m) / jnp.sqrt(s + eps)).reshape(v.shape)

    def _ln_c(v, eps=1e-6):
        m = jnp.mean(v, axis=1, keepdims=True)
        s = jnp.var(v, axis=1, keepdims=True)
        return (v - m) / jnp.sqrt(s + eps)

    def _ln_t(v, eps=1e-5):
        m = jnp.mean(v, axis=-1, keepdims=True)
        s = jnp.var(v, axis=-1, keepdims=True)
        return (v - m) / jnp.sqrt(s + eps)

    def _to_tokens(v):
        B_, C_, H_, W_ = v.shape
        return v.reshape(B_, C_, H_ * W_).transpose(0, 2, 1)
    def _from_tokens(t, like):
        B_, C_, H_, W_ = like.shape
        return t.transpose(0, 2, 1).reshape(B_, C_, H_, W_)

    x = _L0_conv_ref(x, L0_conv_g_w, L0_conv_g_b, L0_conv_theta_w, L0_conv_theta_b, L0_conv_w_w, L0_conv_w_b)
    return x


_drawn_inputs = setup_inputs


def setup_inputs(seed=0):
    import zlib

    import numpy as np

    out = dict(_drawn_inputs(seed))
    spreads = {}
    factors = {'L0_conv_g_b': 8.0, 'L0_conv_theta_w': 64.0, 'L0_conv_theta_b': 64.0}
    for name, (base, spread) in spreads.items():
        noise = np.random.default_rng([zlib.crc32(name.encode()), seed]).standard_normal(out[name].shape)
        drawn = base * np.exp(spread * noise) if base else spread * noise
        out[name] = jnp.asarray(drawn.astype(out[name].dtype))
    for name, factor in factors.items():
        out[name] = (out[name] * factor).astype(out[name].dtype)
    return out
```

```python
import concourse.bass as bass
from concourse import mybir
from contextlib import ExitStack


def covariance_attention_kernel(
    nc: bass.Bass,
    x: bass.AP,
    theta_wT: bass.AP,
    theta_b: bass.AP,
    g_wT: bass.AP,
    g_b: bass.AP,
    w_wT: bass.AP,
    w_b: bass.AP,
    out: bass.AP,
):
    fp32 = mybir.dt.float32
    fp32r = mybir.dt.float32r
    ALU = mybir.AluOpType
    ACT = mybir.ActivationFunctionType
    AX = mybir.AxisListType

    P = 128
    IMAGES, C, M = x.shape
    IC = theta_wT.shape[1]
    KB = C // P
    BANK = 512
    CHUNK = BANK
    QUADS = P // IC
    TILE = QUADS * CHUNK
    TILES = M // TILE
    PAIR = 2 * CHUNK
    PAIRS = TILE // PAIR
    STAGES = 4
    STORE_LAG = 2
    PHASE1_LAG = 2
    ADDS = PAIRS * KB
    TURNS = TILES // STAGES
    SOFTMAX_SCALE = 1.0 / (M * float(IC) ** 0.5)

    x_tiles = x.rearrange("b (k p) m -> b p k m", p=P)
    out_tiles = out.rearrange("b (k p) m -> b p k m", p=P)

    ctx = ExitStack()
    with ctx:
        def sb(name, shape, dt=fp32):
            return ctx.enter_context(nc.sbuf_tensor(name, shape, dt))

        def sem(name):
            return ctx.enter_context(nc.semaphore(name))

        x_sb = sb("x_sb", [P, TILES, KB, TILE])
        stage = sb("stage", [P, STAGES, KB, TILE])
        y_split = sb("y_split", [P, 2, 2, CHUNK], fp32r)
        t_sb = sb("t_sb", [P, CHUNK])
        GROUPS = CHUNK // P
        tT = sb("tT", [P, GROUPS, P + 2])
        v_split = sb("v_split", [P, C], fp32r)
        theta_sb = sb("theta_sb", [P, KB, IC])
        g_sb = sb("g_sb", [P, KB, 2 * IC])
        w_sb = sb("w_sb", [IC, C])
        ident = sb("ident", [P, P])
        fold = sb("fold", [P, IC])
        theta_bias = sb("theta_bias", [P, 1])
        g_bias = sb("g_bias", [P, 1])
        w_bias = sb("w_bias", [P, KB])
        moments = t_sb[:, 0:P + 1]
        neg_mean_row = t_sb[0:IC, 132:132 + IC]
        cov = t_sb[0:IC, 164:164 + IC]
        exps = t_sb[0:IC, 196:196 + IC]
        neg_max = t_sb[0:IC, 228:229]
        row_sum = t_sb[0:IC, 229:230]
        row_recip = t_sb[0:IC, 230:231]
        row_max = t_sb[0:IC, 231:232]
        attn4 = t_sb[0:IC, 256:256 + P]

        ps_out = ctx.enter_context(nc.psum_tensor("ps_out", [P, KB, PAIR], fp32))
        ps_y = ctx.enter_context(nc.psum_tensor("ps_y", [P, 2, CHUNK], fp32))
        ps_t = ctx.enter_context(nc.psum_tensor("ps_t", [P, CHUNK], fp32))
        ps_s = ctx.enter_context(nc.psum_tensor("ps_s", [P, BANK], fp32))
        ps_moments = ps_s[:, 0:P + 1]
        ps_second = ps_s[0:IC, 132:132 + IC]
        ps_row = ps_s[0:IC, 164:164 + IC]
        ps_col = ps_s[0:IC, 196:197]
        ps_v = ps_s[:, 256:256 + C]

        x_loaded = [sem(f"x_loaded{n}") for n in range(TILES)]
        stored = [sem(f"stored{n}") for n in range(STAGES)]
        weights_loaded = sem("weights_loaded")
        zeroed = sem("zeroed")
        ident_ready = sem("ident_ready")
        constants_ready = sem("constants_ready")
        theta_done = sem("theta_done")
        t_copied = sem("t_copied")
        t_turned = sem("t_turned")
        moments_added = sem("moments_added")
        moments_copied = sem("moments_copied")
        moments_folded = sem("moments_folded")
        stage_step = sem("stage_step")
        scores_ready = sem("scores_ready")
        exp_done = sem("exp_done")
        attn_ready = sem("attn_ready")
        v_done = sem("v_done")
        v_ready = sem("v_ready")
        y_done = sem("y_done")
        high_ready = sem("high_ready")
        low_ready = sem("low_ready")
        wy_done = sem("wy_done")
        out_ready = sem("out_ready")
        DVE_STEPS = 6

        weight_loads = [(theta_wT.rearrange("(k p) i -> p k i", p=P), theta_sb[:])]
        weight_loads += [(g_wT.rearrange("(k p) i -> p k i", p=P), g_sb[:, :, bass.ts(c, IC)]) for c in range(2)]
        weight_loads += [(theta_b, theta_bias[bass.ts(q, IC), :]) for q in range(QUADS)]
        weight_loads += [(g_b, g_bias[bass.ts(q, IC), :]) for q in range(QUADS)]
        weight_loads += [(w_b[bass.ts(k, P), :], w_bias[:, k:k + 1]) for k in range(KB)]
        weight_loads += [(w_wT, w_sb[:])]
        WEIGHT_LOADS = len(weight_loads)

        block = ctx.enter_context(nc.Block())

        @block.sync
        def _(sp):
            def load(image, j):
                sp.dma_start(x_sb[:, j], x_tiles[image, :, :, bass.ts(j, TILE)]).then_inc(x_loaded[j], 16)

            def store(image, j):
                sp.dma_start(out_tiles[image, :, :, bass.ts(j, TILE)], stage[:, j % STAGES])\
                  .then_inc(stored[j % STAGES], 16)

            for j in range(TILES):
                load(0, j)
            with sp.Fori(0, IMAGES - 1) as image:
                for j in range(TILES):
                    sp.wait_ge(out_ready, image * (TILES * ADDS) + (j + 1) * ADDS)
                    load(image + 1, j)
                    if j >= STORE_LAG:
                        store(image, j - STORE_LAG)
                for j in range(TILES - STORE_LAG, TILES):
                    store(image, j)
            for j in range(TILES):
                sp.wait_ge(out_ready, ((IMAGES - 1) * TILES + j + 1) * ADDS)
                store(IMAGES - 1, j)
            for n in range(STAGES):
                sp.wait_ge(stored[n], 16 * TURNS * IMAGES)

        @block.gpsimd
        def _(pool):
            pool.memset(ident[:], 0.0).then_inc(zeroed, 1)
            pool.wait_ge(zeroed, 1)
            pool.affine_select(out=ident[:], in_=ident[:], compare_op=ALU.not_equal, fill=1.0, base=0,
                               pattern=[[-1, P]], channel_multiplier=1).then_inc(ident_ready, 1)

        @block.tensor
        def _(pe):
            def theta(image, n):
                pe.wait_ge(x_loaded[n], (image + 1) * 16)
                if not (n == 0 and type(image) is int and image == 0):
                    pe.wait_ge(t_copied, image * TILES + n)
                for k in range(KB):
                    for q in range(QUADS):
                        mm = pe.matmul(ps_t[q * IC:(q + 1) * IC, :], theta_sb[:, k, :],
                                       x_sb[:, n, k, bass.ts(q, CHUNK)], start=(k == 0), stop=(k == KB - 1))
                mm.then_inc(theta_done, 1)

            def moments_of(image, n):
                pe.wait_ge(t_turned, image * TILES + (n + 1))
                for a in range(GROUPS):
                    mm = pe.matmul(ps_moments, tT[:, a, 0:P], tT[:, a, 0:P + 1],
                                   start=(n == 0 and a == 0), stop=(n == TILES - 1 and a == GROUPS - 1))
                mm.then_inc(moments_added, 1)

            def project(j, h):
                for k in range(KB):
                    for c in range(2):
                        mm = pe.matmul(ps_y[2 * c * IC:2 * (c + 1) * IC, h % 2, :], g_sb[:, k, :],
                                       x_sb[:, j, k, bass.ts(2 * h + c, CHUNK)],
                                       start=(k == 0), stop=(k == KB - 1))
                mm.then_inc(y_done, 1)

            def expand(image, j, h):
                pair = j * PAIRS + h
                pe.wait_ge(low_ready, image * (2 * PAIRS * TILES) + 2 * (pair + 1))
                for k in range(KB):
                    if pair > 0:
                        pe.wait_ge(out_ready, image * (TILES * ADDS) + (pair - 1) * KB + k + 1)
                    for c in range(2):
                        mm = pe.matmul(ps_out[:, k, bass.ts(c, CHUNK)], v_split[:, bass.ts(k, P)],
                                       y_split[:, h % 2, c, :], start=True, stop=True)
                    mm.then_inc(wy_done, 1)

            def attention(image):
                pe.wait_ge(moments_copied, image + 1)
                for q in range(QUADS):
                    pe.matmul(ps_second, ident[:, bass.ts(q, IC)], moments[:, bass.ts(q, IC)],
                              start=(q == 0), stop=(q == QUADS - 1))
                pe.matmul(ps_row, moments[:, P:P + 1].to_broadcast([P, IC]), fold[:], start=True, stop=True)
                pe.matmul(ps_col, fold[:], moments[:, P:P + 1], start=True, stop=True).then_inc(moments_folded, 1)
                project(0, 0)
                pe.wait_ge(attn_ready, image + 1)
                pe.matmul(ps_v, attn4, w_sb[:], start=True, stop=True).then_inc(v_done, 1)

            def phase2_tile(image, j, n=None, next_image=None):
                if n is not None:
                    theta(next_image, n)
                for h in range(PAIRS):
                    if h + 1 < PAIRS:
                        project(j, h + 1)
                    elif j + 1 < TILES:
                        project(j + 1, 0)
                    if j == 0 and h == 0:
                        pe.wait_ge(v_ready, image + 1)
                    expand(image, j, h)
                if n is not None:
                    moments_of(next_image, n)

            pe.wait_ge(weights_loaded, WEIGHT_LOADS * 16)
            pe.wait_ge(constants_ready, 2)
            for n in range(TILES):
                theta(0, n)
                moments_of(0, n)
            attention(0)
            with pe.Fori(0, IMAGES - 1) as image:
                for j in range(TILES):
                    if j < PHASE1_LAG:
                        phase2_tile(image, j)
                    else:
                        phase2_tile(image, j, j - PHASE1_LAG, image + 1)
                for n in range(TILES - PHASE1_LAG, TILES):
                    theta(image + 1, n)
                    moments_of(image + 1, n)
                attention(image + 1)
            for j in range(TILES):
                phase2_tile(IMAGES - 1, j)

        @block.scalar
        def _(act):
            for src, dst in weight_loads:
                act.dma_start(dst, src).then_inc(weights_loaded, 16)
            act.wait_ge(weights_loaded, WEIGHT_LOADS * 16)

            def copy_t(image, n):
                act.wait_ge(theta_done, image * TILES + (n + 1))
                if not (n == 0 and type(image) is int and image == 0):
                    act.wait_ge(t_turned, image * TILES + n)
                act.activation(t_sb[:], ps_t[:], ACT.Identity, bias=theta_bias[:]).then_inc(t_copied, 1)

            def split_high(image, j, h):
                pair = j * PAIRS + h
                act.wait_ge(y_done, image * (PAIRS * TILES) + (pair + 1))
                if pair >= 2:
                    act.wait_ge(wy_done, image * (TILES * ADDS) + (pair - 1) * KB)
                for c in range(2):
                    rows = slice(2 * c * IC, 2 * (c + 1) * IC)
                    act.activation(y_split[rows, h % 2, c, :], ps_y[rows, h % 2, :], ACT.Identity,
                                   bias=g_bias[rows, :]).then_inc(high_ready, 1)

            def attention(image):
                act.wait_ge(moments_added, image * TILES + TILES)
                act.activation(moments, ps_moments, ACT.Copy).then_inc(moments_copied, 1)
                split_high(image, 0, 0)
                act.wait_ge(scores_ready, image + 1)
                act.activation(exps, cov, ACT.Exp, bias=neg_max, scale=SOFTMAX_SCALE,
                               accum_out=row_sum).then_inc(exp_done, 1)

            def phase2_tile(image, j, n=None, next_image=None):
                if n is not None:
                    copy_t(next_image, n)
                for h in range(PAIRS):
                    if h + 1 < PAIRS:
                        split_high(image, j, h + 1)
                    elif j + 1 < TILES:
                        split_high(image, j + 1, 0)

            for n in range(TILES):
                copy_t(0, n)
            attention(0)
            with act.Fori(0, IMAGES - 1) as image:
                for j in range(TILES):
                    if j < PHASE1_LAG:
                        phase2_tile(image, j)
                    else:
                        phase2_tile(image, j, j - PHASE1_LAG, image + 1)
                for n in range(TILES - PHASE1_LAG, TILES):
                    copy_t(image + 1, n)
                attention(image + 1)
            for j in range(TILES):
                phase2_tile(IMAGES - 1, j)

        @block.vector
        def _(dve):
            def turn_t(image, n):
                dve.wait_ge(t_copied, image * TILES + (n + 1))
                if not (n == 0 and type(image) is int and image == 0):
                    dve.wait_ge(moments_added, image * TILES + n)
                dve.transpose(tT[:, :, 0:P], t_sb[:].rearrange("p (a c) -> p a c", c=P)).then_inc(t_turned, 1)

            def split_low(image, j, h):
                pair = j * PAIRS + h
                for c in range(2):
                    rows = slice(2 * c * IC, 2 * (c + 1) * IC)
                    others = slice(2 * (1 - c) * IC, 2 * (2 - c) * IC)
                    dve.wait_ge(high_ready, image * (2 * PAIRS * TILES) + (2 * pair + c + 1))
                    dve.scalar_tensor_tensor(out=y_split[others, h % 2, c, :], in0=ps_y[rows, h % 2, :],
                                             scalar=g_bias[rows, :], in1=y_split[rows, h % 2, c, :].bitcast(fp32),
                                             op0=ALU.add, op1=ALU.subtract).then_inc(low_ready, 1)

            def add_out(image, j, h):
                pair = j * PAIRS + h
                for k in range(KB):
                    dve.wait_ge(wy_done, image * (TILES * ADDS) + (pair * KB + k + 1))
                    dve.scalar_tensor_tensor(out=stage[:, j % STAGES, k, bass.ts(h, PAIR)], in0=ps_out[:, k, :],
                                             scalar=w_bias[:, k:k + 1], in1=x_sb[:, j, k, bass.ts(h, PAIR)],
                                             op0=ALU.add, op1=ALU.add).then_inc(out_ready, 1)

            def attention(image):
                steps = [0]

                def step(instruction):
                    steps[0] += 1
                    instruction.then_inc(stage_step, 1)
                    dve.wait_ge(stage_step, image * DVE_STEPS + steps[0])

                split_low(image, 0, 0)
                dve.wait_ge(moments_folded, image + 1)
                step(dve.tensor_scalar(neg_mean_row, ps_row, -1.0 / M, None, ALU.mult))
                step(dve.scalar_tensor_tensor(out=cov, in0=neg_mean_row, scalar=ps_col, in1=ps_second,
                                              op0=ALU.mult, op1=ALU.add))
                step(dve.tensor_reduce(row_max, cov, AX.X, ALU.max))
                dve.tensor_scalar(neg_max, row_max, -SOFTMAX_SCALE, None, ALU.mult).then_inc(scores_ready, 1)
                dve.wait_ge(exp_done, image + 1)
                step(dve.reciprocal(row_recip, row_sum))
                dve.tensor_scalar(attn4.rearrange("p (q c) -> p q c", q=QUADS),
                                  exps.unsqueeze(1).to_broadcast([IC, QUADS, IC]), row_recip, None,
                                  ALU.mult).then_inc(attn_ready, 1)
                dve.wait_ge(v_done, image + 1)
                step(dve.tensor_copy(v_split[:], ps_v))
                for q in range(1, QUADS, 2):
                    rows = slice(q * IC, (q + 1) * IC)
                    low = dve.tensor_tensor(v_split[rows, :], ps_v[rows, :], v_split[rows, :].bitcast(fp32),
                                            ALU.subtract)
                    if q + 2 < QUADS:
                        low.then_inc(stage_step, 1)
                        steps[0] += 1
                low.then_inc(v_ready, 1)
                assert steps[0] == DVE_STEPS

            def phase2_tile(image, j, n=None, next_image=None):
                for h in range(PAIRS):
                    if h + 1 < PAIRS:
                        split_low(image, j, h + 1)
                    elif j + 1 < TILES:
                        split_low(image, j + 1, 0)
                    if h == 0:
                        turn = j // STAGES
                        if not (turn == 0 and type(image) is int and image == 0):
                            dve.wait_ge(stored[j % STAGES], image * (16 * TURNS) + 16 * turn)
                    add_out(image, j, h)
                    if n is not None and h == 0:
                        turn_t(next_image, n)

            dve.memset(tT[:], 1.0).then_inc(constants_ready, 1)
            dve.wait_ge(ident_ready, 1)
            dve.tensor_reduce(fold[:], ident[:].rearrange("p (q c) -> p c q", q=QUADS), AX.X, ALU.add)\
               .then_inc(constants_ready, 1)
            dve.wait_ge(constants_ready, 2)
            dve.wait_ge(weights_loaded, WEIGHT_LOADS * 16)
            for n in range(TILES):
                turn_t(0, n)
            attention(0)
            with dve.Fori(0, IMAGES - 1) as image:
                for j in range(TILES):
                    if j < PHASE1_LAG:
                        phase2_tile(image, j)
                    else:
                        phase2_tile(image, j, j - PHASE1_LAG, image + 1)
                for n in range(TILES - PHASE1_LAG, TILES):
                    turn_t(image + 1, n)
                attention(image + 1)
            for j in range(TILES):
                phase2_tile(IMAGES - 1, j)


def kernel(x, L0_conv_g_w, L0_conv_g_b, L0_conv_theta_w, L0_conv_theta_b, L0_conv_w_w, L0_conv_w_b):
    import numpy as _np
    import concourse.bacc as _bacc
    from concourse import mybir as _mybir
    from concourse.bass_utils import run_bass_kernel_spmd as _run

    B, C, H, W = x.shape
    given = {
        "x": _np.asarray(x).reshape(B, C, H * W),
        "theta_wT": _np.ascontiguousarray(_np.asarray(L0_conv_theta_w).T),
        "theta_b": _np.asarray(L0_conv_theta_b).reshape(-1, 1),
        "g_wT": _np.ascontiguousarray(_np.asarray(L0_conv_g_w).T),
        "g_b": _np.asarray(L0_conv_g_b).reshape(-1, 1),
        "w_wT": _np.ascontiguousarray(_np.asarray(L0_conv_w_w).T),
        "w_b": _np.asarray(L0_conv_w_b).reshape(-1, 1),
    }
    nc = _bacc.Bacc("TRN2", target_bir_lowering=False, num_devices=1)
    arrays, args = {}, []
    for name, a in given.items():
        arrays[f"in_{name}_dram"] = a
        args.append(nc.dram_tensor(f"in_{name}_dram", a.shape, _mybir.dt.from_np(a.dtype), kind="ExternalInput").ap())
    args.append(nc.dram_tensor("out_dram", (B, C, H * W), _mybir.dt.float32, kind="ExternalOutput").ap())
    covariance_attention_kernel(nc, *args)
    r = _run(nc, [arrays], core_ids=[0])
    return r.results[0]["out_dram"].reshape(B, C, H, W)
```

```python
import concourse.bass as bass
from concourse import mybir
from contextlib import ExitStack


def covariance_attention_kernel(
    nc: bass.Bass,
    x: bass.AP,
    weights: bass.AP,
    w_wT: bass.AP,
    out: bass.AP,
):
    fp32 = mybir.dt.float32
    fp32r = mybir.dt.float32r
    ALU = mybir.AluOpType
    ACT = mybir.ActivationFunctionType
    AX = mybir.AxisListType

    P = 128
    IMAGES, C, M = x.shape
    IC = w_wT.shape[0]
    KB = C // P
    BANK = 512
    CHUNK = BANK
    QUADS = P // IC
    PAIR = 2 * CHUNK
    PAIRS = M // PAIR
    TILE = QUADS * CHUNK
    TILE_PAIRS = TILE // PAIR
    TILES = M // TILE
    STAGES = 8
    TURNS = PAIRS // STAGES
    PHASE1_LAG = 3
    STORE_AFTER = [p - min(p // 2, 5) for p in range(PAIRS - 1)] + [PAIRS - 1]
    SOFTMAX_SCALE = 1.0 / (M * float(IC) ** 0.5)

    x_blocks = x.rearrange("b (k p) m -> b p k m", p=P)
    out_blocks = out.rearrange("b (k p) m -> b p k m", p=P)

    ctx = ExitStack()
    with ctx:
        def sb(name, shape, dt=fp32):
            return ctx.enter_context(nc.sbuf_tensor(name, shape, dt))

        def sem(name):
            return ctx.enter_context(nc.semaphore(name))

        x_sb = sb("x_sb", [P, PAIRS, KB, PAIR])
        stage = sb("stage", [P, STAGES, KB, PAIR])
        y_split = sb("y_split", [P, 2, 2, CHUNK], fp32r)
        t_sb = sb("t_sb", [P, CHUNK])
        GROUPS = CHUNK // P
        tT = sb("tT", [P, GROUPS, P + 2])
        v_split = sb("v_split", [P, C], fp32r)
        weights_sb = sb("weights_sb", [P, weights.shape[1]])
        theta_sb = weights_sb[:, 0:KB * IC].rearrange("p (k i) -> p k i", k=KB)
        g_sb = weights_sb[:, KB * IC:3 * KB * IC].rearrange("p (k i) -> p k i", k=KB)
        theta_bias = weights_sb[:, 3 * KB * IC:3 * KB * IC + 1]
        g_bias = weights_sb[:, 3 * KB * IC + 1:3 * KB * IC + 2]
        w_bias = weights_sb[:, 3 * KB * IC + 2:3 * KB * IC + 2 + KB]
        w_sb = sb("w_sb", [IC, C])
        ident = sb("ident", [P, P])
        fold = sb("fold", [P, IC])
        moments = t_sb[:, 0:P + 1]
        neg_mean_row = t_sb[0:IC, 132:132 + IC]
        cov = t_sb[0:IC, 164:164 + IC]
        exps = t_sb[0:IC, 196:196 + IC]
        neg_max = t_sb[0:IC, 228:229]
        row_sum = t_sb[0:IC, 229:230]
        row_recip = t_sb[0:IC, 230:231]
        row_max = t_sb[0:IC, 231:232]
        attn4 = t_sb[0:IC, 256:256 + P]

        ps_out = ctx.enter_context(nc.psum_tensor("ps_out", [P, KB, PAIR], fp32))
        ps_y = ctx.enter_context(nc.psum_tensor("ps_y", [P, 2, CHUNK], fp32))
        ps_t = ctx.enter_context(nc.psum_tensor("ps_t", [P, CHUNK], fp32))
        ps_s = ctx.enter_context(nc.psum_tensor("ps_s", [P, BANK], fp32))
        ps_moments = ps_s[:, 0:P + 1]
        ps_second = ps_s[0:IC, 132:132 + IC]
        ps_row = ps_s[0:IC, 164:164 + IC]
        ps_col = ps_s[0:IC, 196:197]
        ps_v = ps_s[:, 256:256 + C]

        x_loaded = [sem(f"x_loaded{n}") for n in range(PAIRS)]
        stored = [sem(f"stored{n}") for n in range(STAGES)]
        weights_loaded = sem("weights_loaded")
        zeroed = sem("zeroed")
        ident_ready = sem("ident_ready")
        constants_ready = sem("constants_ready")
        theta_done = sem("theta_done")
        t_copied = sem("t_copied")
        t_turned = sem("t_turned")
        moments_added = sem("moments_added")
        moments_copied = sem("moments_copied")
        moments_folded = sem("moments_folded")
        stage_step = sem("stage_step")
        scores_ready = sem("scores_ready")
        exp_done = sem("exp_done")
        attn_ready = sem("attn_ready")
        v_done = sem("v_done")
        v_high_ready = sem("v_high_ready")
        v_ready = sem("v_ready")
        y_done = sem("y_done")
        high_ready = sem("high_ready")
        low_ready = sem("low_ready")
        wy_done = sem("wy_done")
        out_ready = sem("out_ready")
        DVE_STEPS = 4

        block = ctx.enter_context(nc.Block())

        @block.sync
        def _(sp):
            def load(image, p):
                sp.dma_start(x_sb[:, p], x_blocks[image, :, :, bass.ts(p, PAIR)]).then_inc(x_loaded[p], 16)

            def store(image, p):
                sp.dma_start(out_blocks[image, :, :, bass.ts(p, PAIR)], stage[:, p % STAGES])\
                  .then_inc(stored[p % STAGES], 16)

            def traffic(image):
                stores = 0
                for p in range(PAIRS):
                    sp.wait_ge(out_ready, image * (PAIRS * KB) + (p + 1) * KB)
                    load(image + 1, p)
                    while stores <= STORE_AFTER[p]:
                        store(image, stores)
                        stores += 1

            sp.dma_start(weights_sb[:], weights).then_inc(weights_loaded, 16)
            sp.dma_start(w_sb[:], w_wT).then_inc(weights_loaded, 16)
            for p in range(PAIRS):
                load(0, p)
            traffic(0)
            with sp.Fori(1, IMAGES - 1) as image:
                traffic(image)
            for p in range(PAIRS):
                sp.wait_ge(out_ready, ((IMAGES - 1) * PAIRS + p + 1) * KB)
                store(IMAGES - 1, p)
            for n in range(STAGES):
                sp.wait_ge(stored[n], 16 * TURNS * IMAGES)

        @block.gpsimd
        def _(pool):
            pool.memset(ident[:], 0.0).then_inc(zeroed, 1)
            pool.wait_ge(zeroed, 1)
            pool.affine_select(out=ident[:], in_=ident[:], compare_op=ALU.not_equal, fill=1.0, base=0,
                               pattern=[[-1, P]], channel_multiplier=1).then_inc(ident_ready, 1)

        @block.tensor
        def _(pe):
            def theta(image, n):
                for p in range(TILE_PAIRS * n, TILE_PAIRS * (n + 1)):
                    pe.wait_ge(x_loaded[p], (image + 1) * 16)
                if not (n == 0 and type(image) is int and image == 0):
                    pe.wait_ge(t_copied, image * TILES + n)
                for k in range(KB):
                    for q in range(QUADS):
                        mm = pe.matmul(ps_t[q * IC:(q + 1) * IC, :], theta_sb[:, k, :],
                                       x_sb[:, TILE_PAIRS * n + q // 2, k, bass.ts(q % 2, CHUNK)],
                                       start=(k == 0), stop=(k == KB - 1))
                mm.then_inc(theta_done, 1)

            def moments_of(image, n):
                pe.wait_ge(t_turned, image * TILES + (n + 1))
                for a in range(GROUPS):
                    mm = pe.matmul(ps_moments, tT[:, a, 0:P], tT[:, a, 0:P + 1],
                                   start=(n == 0 and a == 0), stop=(n == TILES - 1 and a == GROUPS - 1))
                mm.then_inc(moments_added, 1)

            def project(p):
                for k in range(KB):
                    for c in range(2):
                        mm = pe.matmul(ps_y[2 * c * IC:2 * (c + 1) * IC, p % 2, :], g_sb[:, k, :],
                                       x_sb[:, p, k, bass.ts(c, CHUNK)], start=(k == 0), stop=(k == KB - 1))
                mm.then_inc(y_done, 1)

            def expand(image, p):
                pe.wait_ge(low_ready, image * (2 * PAIRS) + 2 * (p + 1))
                if p == 0:
                    pe.wait_ge(v_ready, image + 1)
                for k in range(KB):
                    if p > 0:
                        pe.wait_ge(out_ready, image * (PAIRS * KB) + (p - 1) * KB + k + 1)
                    for c in range(2):
                        mm = pe.matmul(ps_out[:, k, bass.ts(c, CHUNK)], v_split[:, bass.ts(k, P)],
                                       y_split[:, p % 2, c, :], start=True, stop=True)
                    mm.then_inc(wy_done, 1)

            def attention(image):
                pe.wait_ge(moments_copied, image + 1)
                for q in range(QUADS):
                    pe.matmul(ps_second, ident[:, bass.ts(q, IC)], moments[:, bass.ts(q, IC)],
                              start=(q == 0), stop=(q == QUADS - 1))
                pe.matmul(ps_row, moments[:, P:P + 1].to_broadcast([P, IC]), fold[:], start=True, stop=True)
                pe.matmul(ps_col, fold[:], moments[:, P:P + 1], start=True, stop=True).then_inc(moments_folded, 1)
                project(0)
                pe.wait_ge(attn_ready, image + 1)
                pe.matmul(ps_v, attn4, w_sb[:], start=True, stop=True).then_inc(v_done, 1)

            def phase2(image, p):
                if p + 1 < PAIRS:
                    project(p + 1)
                expand(image, p)

            def both_phases(image):
                for j in range(TILES):
                    if j >= PHASE1_LAG:
                        theta(image + 1, j - PHASE1_LAG)
                    for p in range(TILE_PAIRS * j, TILE_PAIRS * (j + 1)):
                        phase2(image, p)
                    if j >= PHASE1_LAG:
                        moments_of(image + 1, j - PHASE1_LAG)
                for n in range(TILES - PHASE1_LAG, TILES):
                    theta(image + 1, n)
                    moments_of(image + 1, n)
                attention(image + 1)

            pe.wait_ge(weights_loaded, 2 * 16)
            pe.wait_ge(constants_ready, 2)
            for n in range(TILES):
                theta(0, n)
                moments_of(0, n)
            attention(0)
            both_phases(0)
            with pe.Fori(1, IMAGES - 1) as image:
                both_phases(image)
            for p in range(PAIRS):
                phase2(IMAGES - 1, p)

        @block.scalar
        def _(act):
            def copy_t(image, n):
                act.wait_ge(theta_done, image * TILES + (n + 1))
                if not (n == 0 and type(image) is int and image == 0):
                    act.wait_ge(t_turned, image * TILES + n)
                act.activation(t_sb[:], ps_t[:], ACT.Identity, bias=theta_bias[:]).then_inc(t_copied, 1)

            def split_high(image, p):
                act.wait_ge(y_done, image * PAIRS + (p + 1))
                if p >= 2:
                    act.wait_ge(wy_done, image * (PAIRS * KB) + (p - 1) * KB)
                for c in range(2):
                    rows = slice(2 * c * IC, 2 * (c + 1) * IC)
                    act.activation(y_split[rows, p % 2, c, :], ps_y[rows, p % 2, :], ACT.Identity,
                                   bias=g_bias[rows, :]).then_inc(high_ready, 1)

            def attention(image):
                act.wait_ge(moments_added, image * TILES + TILES)
                act.activation(moments, ps_moments, ACT.Copy).then_inc(moments_copied, 1)
                act.wait_ge(scores_ready, image + 1)
                act.activation(exps, cov, ACT.Exp, bias=neg_max, scale=SOFTMAX_SCALE,
                               accum_out=row_sum).then_inc(exp_done, 1)
                split_high(image, 0)
                act.wait_ge(v_done, image + 1)
                act.activation(v_split[:], ps_v, ACT.Copy).then_inc(v_high_ready, 1)

            def both_phases(image):
                for j in range(TILES):
                    if j >= PHASE1_LAG:
                        copy_t(image + 1, j - PHASE1_LAG)
                    for p in range(TILE_PAIRS * j + 1, min(TILE_PAIRS * (j + 1) + 1, PAIRS)):
                        split_high(image, p)
                for n in range(TILES - PHASE1_LAG, TILES):
                    copy_t(image + 1, n)
                attention(image + 1)

            act.wait_ge(weights_loaded, 2 * 16)
            for n in range(TILES):
                copy_t(0, n)
            attention(0)
            both_phases(0)
            with act.Fori(1, IMAGES - 1) as image:
                both_phases(image)
            for p in range(1, PAIRS):
                split_high(IMAGES - 1, p)

        @block.vector
        def _(dve):
            def turn_t(image, n):
                dve.wait_ge(t_copied, image * TILES + (n + 1))
                if not (n == 0 and type(image) is int and image == 0):
                    dve.wait_ge(moments_added, image * TILES + n)
                dve.transpose(tT[:, :, 0:P], t_sb[:].rearrange("p (a c) -> p a c", c=P)).then_inc(t_turned, 1)

            def split_low(image, p):
                for c in range(2):
                    rows = slice(2 * c * IC, 2 * (c + 1) * IC)
                    others = slice(2 * (1 - c) * IC, 2 * (2 - c) * IC)
                    dve.wait_ge(high_ready, image * (2 * PAIRS) + (2 * p + c + 1))
                    dve.scalar_tensor_tensor(out=y_split[others, p % 2, c, :], in0=ps_y[rows, p % 2, :],
                                             scalar=g_bias[rows, :], in1=y_split[rows, p % 2, c, :].bitcast(fp32),
                                             op0=ALU.add, op1=ALU.subtract).then_inc(low_ready, 1)

            def add_out(image, p):
                turn = p // STAGES
                if not (turn == 0 and type(image) is int and image == 0):
                    dve.wait_ge(stored[p % STAGES], image * (16 * TURNS) + 16 * turn)
                for k in range(KB):
                    dve.wait_ge(wy_done, image * (PAIRS * KB) + (p * KB + k + 1))
                    dve.scalar_tensor_tensor(out=stage[:, p % STAGES, k, :], in0=ps_out[:, k, :],
                                             scalar=w_bias[:, k:k + 1], in1=x_sb[:, p, k, :],
                                             op0=ALU.add, op1=ALU.add).then_inc(out_ready, 1)

            def attention(image):
                steps = [0]

                def step(instruction):
                    steps[0] += 1
                    instruction.then_inc(stage_step, 1)
                    dve.wait_ge(stage_step, image * DVE_STEPS + steps[0])

                dve.wait_ge(moments_folded, image + 1)
                step(dve.tensor_scalar(neg_mean_row, ps_row, -1.0 / M, None, ALU.mult))
                step(dve.scalar_tensor_tensor(out=cov, in0=neg_mean_row, scalar=ps_col, in1=ps_second,
                                              op0=ALU.mult, op1=ALU.add))
                step(dve.tensor_reduce(row_max, cov, AX.X, ALU.max))
                dve.tensor_scalar(neg_max, row_max, -SOFTMAX_SCALE, None, ALU.mult).then_inc(scores_ready, 1)
                dve.wait_ge(exp_done, image + 1)
                step(dve.reciprocal(row_recip, row_sum))
                dve.tensor_scalar(attn4.rearrange("p (q c) -> p q c", q=QUADS),
                                  exps.unsqueeze(1).to_broadcast([IC, QUADS, IC]), row_recip, None,
                                  ALU.mult).then_inc(attn_ready, 1)
                split_low(image, 0)
                dve.wait_ge(v_high_ready, image + 1)
                for q in range(1, QUADS, 2):
                    rows = slice(q * IC, (q + 1) * IC)
                    low = dve.tensor_tensor(v_split[rows, :], ps_v[rows, :], v_split[rows, :].bitcast(fp32),
                                            ALU.subtract)
                low.then_inc(v_ready, 1)
                assert steps[0] == DVE_STEPS

            def phase2(image, p):
                if p + 1 < PAIRS:
                    split_low(image, p + 1)
                add_out(image, p)

            def both_phases(image):
                for j in range(TILES):
                    for p in range(TILE_PAIRS * j, TILE_PAIRS * (j + 1)):
                        phase2(image, p)
                        if j >= PHASE1_LAG and p == TILE_PAIRS * j:
                            turn_t(image + 1, j - PHASE1_LAG)
                for n in range(TILES - PHASE1_LAG, TILES):
                    turn_t(image + 1, n)
                attention(image + 1)

            dve.memset(tT[:], 1.0).then_inc(constants_ready, 1)
            dve.wait_ge(ident_ready, 1)
            dve.tensor_reduce(fold[:], ident[:].rearrange("p (q c) -> p c q", q=QUADS), AX.X, ALU.add)\
               .then_inc(constants_ready, 1)
            dve.wait_ge(constants_ready, 2)
            dve.wait_ge(weights_loaded, 2 * 16)
            for n in range(TILES):
                turn_t(0, n)
            attention(0)
            both_phases(0)
            with dve.Fori(1, IMAGES - 1) as image:
                both_phases(image)
            for p in range(PAIRS):
                phase2(IMAGES - 1, p)


def kernel(x, L0_conv_g_w, L0_conv_g_b, L0_conv_theta_w, L0_conv_theta_b, L0_conv_w_w, L0_conv_w_b):
    import numpy as _np
    import concourse.bacc as _bacc
    from concourse import mybir as _mybir
    from concourse.bass_utils import run_bass_kernel_spmd as _run

    B, C, H, W = x.shape
    P = 128
    theta_w, g_w, w_w = (_np.asarray(a) for a in (L0_conv_theta_w, L0_conv_g_w, L0_conv_w_w))
    IC = theta_w.shape[0]

    def by_blocks(a):
        return a.reshape(a.shape[0], C // P, P).transpose(2, 1, 0)

    weights = _np.concatenate(
        [
            by_blocks(theta_w).reshape(P, -1),
            by_blocks(_np.concatenate([g_w, g_w])).reshape(P, -1),
            _np.tile(_np.asarray(L0_conv_theta_b), P // IC).reshape(P, 1),
            _np.tile(_np.asarray(L0_conv_g_b), P // IC).reshape(P, 1),
            _np.asarray(L0_conv_w_b).reshape(C // P, P).T,
        ],
        axis=1,
    )
    given = {
        "x": _np.asarray(x).reshape(B, C, H * W),
        "weights": _np.ascontiguousarray(weights),
        "w_wT": _np.ascontiguousarray(w_w.T),
    }
    nc = _bacc.Bacc("TRN2", target_bir_lowering=False, num_devices=1)
    arrays, args = {}, []
    for name, a in given.items():
        arrays[f"in_{name}_dram"] = a
        args.append(nc.dram_tensor(f"in_{name}_dram", a.shape, _mybir.dt.from_np(a.dtype), kind="ExternalInput").ap())
    args.append(nc.dram_tensor("out_dram", (B, C, H * W), _mybir.dt.float32, kind="ExternalOutput").ap())
    covariance_attention_kernel(nc, *args)
    r = _run(nc, [arrays], core_ids=[0])
    return r.results[0]["out_dram"].reshape(B, C, H, W)
```

```python
import concourse.bass as bass
from concourse import mybir
from contextlib import ExitStack


def covariance_attention_kernel(
    nc: bass.Bass,
    x: bass.AP,
    weights: bass.AP,
    w_wT: bass.AP,
    out: bass.AP,
):
    fp32 = mybir.dt.float32
    fp32r = mybir.dt.float32r
    ALU = mybir.AluOpType
    ACT = mybir.ActivationFunctionType
    AX = mybir.AxisListType

    P = 128
    IMAGES, C, M = x.shape
    IC = w_wT.shape[0]
    KB = C // P
    BANK = 512
    CHUNK = BANK
    QUADS = P // IC
    PAIR = 2 * CHUNK
    PAIRS = M // PAIR
    TILE = QUADS * CHUNK
    TILE_PAIRS = TILE // PAIR
    TILES = M // TILE
    LAST = 1
    assert KB == 2
    STAGES = 8
    TURNS = PAIRS // STAGES
    PHASE1_LAG = 3
    def stores_after(image, p):
        if p == PAIRS - 1:
            return p
        if is_first(image):
            return p - max(0, p - STAGES - 1)
        return p - min(p // 2, 6)

    def is_first(image):
        return type(image) is int and image == 0

    def is_early(image, p):
        return is_first(image) and p < STAGES

    def phase1_tile(j):
        return j - PHASE1_LAG if j >= PHASE1_LAG else None

    def early_outputs(p, k):
        return p * KB + k + 1

    def outputs(image, p):
        return image * PAIRS + (p + 1 - STAGES)

    SOFTMAX_SCALE = 1.0 / (M * float(IC) ** 0.5)

    x_blocks = x.rearrange("b (k p) m -> b p k m", p=P)
    out_blocks = out.rearrange("b (k p) m -> b p k m", p=P)

    ctx = ExitStack()
    with ctx:
        def sb(name, shape, dt=fp32):
            return ctx.enter_context(nc.sbuf_tensor(name, shape, dt))

        def sem(name):
            return ctx.enter_context(nc.semaphore(name))

        x_sb = sb("x_sb", [P, PAIRS, KB, PAIR])
        stage = sb("stage", [P, STAGES, KB, PAIR])

        def x_of(image, p):
            return stage[:, p] if is_early(image, p) else x_sb[:, p]

        y_split = sb("y_split", [P, 2, 2, CHUNK], fp32r)
        t_sb = sb("t_sb", [P, CHUNK])
        GROUPS = CHUNK // P
        tT = sb("tT", [P, GROUPS, P + 2])
        v_split = sb("v_split", [P, C], fp32r)
        weights_sb = sb("weights_sb", [P, weights.shape[1]])
        theta_sb = weights_sb[:, 0:KB * IC].rearrange("p (k i) -> p k i", k=KB)
        g_sb = weights_sb[:, KB * IC:3 * KB * IC].rearrange("p (k i) -> p k i", k=KB)
        theta_bias = weights_sb[:, 3 * KB * IC:3 * KB * IC + 1]
        g_bias = weights_sb[:, 3 * KB * IC + 1:3 * KB * IC + 2]
        w_bias = weights_sb[:, 3 * KB * IC + 2:3 * KB * IC + 2 + KB]
        w_sb = sb("w_sb", [IC, C])
        ident = sb("ident", [P, P])
        fold = sb("fold", [P, IC])
        moments = t_sb[:, 0:P + 1]
        neg_mean_row = t_sb[0:IC, 132:132 + IC]
        cov = t_sb[0:IC, 164:164 + IC]
        exps = t_sb[0:IC, 196:196 + IC]
        neg_max = t_sb[0:IC, 228:229]
        row_sum = t_sb[0:IC, 229:230]
        row_recip = t_sb[0:IC, 230:231]
        row_max = t_sb[0:IC, 231:232]
        attn4 = t_sb[0:IC, 256:256 + P]

        ps_out = ctx.enter_context(nc.psum_tensor("ps_out", [P, KB, PAIR], fp32))
        ps_y = ctx.enter_context(nc.psum_tensor("ps_y", [P, 2, CHUNK], fp32))
        ps_t = ctx.enter_context(nc.psum_tensor("ps_t", [P, CHUNK], fp32))
        ps_s = ctx.enter_context(nc.psum_tensor("ps_s", [P, BANK], fp32))
        ps_moments = ps_s[:, 0:P + 1]
        ps_second = ps_s[0:IC, 132:132 + IC]
        ps_row = ps_s[0:IC, 164:164 + IC]
        ps_col = ps_s[0:IC, 196:197]
        ps_v = ps_s[:, 256:256 + C]

        x_loaded = [sem(f"x_loaded{n}") for n in range(PAIRS)]
        x_loaded_early = [sem(f"x_loaded_early{n}") for n in range(STAGES)]
        stored = [sem(f"stored{n}") for n in range(STAGES)]
        weights_loaded = sem("weights_loaded")
        zeroed = sem("zeroed")
        ident_ready = sem("ident_ready")
        constants_ready = sem("constants_ready")
        theta_done = sem("theta_done")
        t_copied = sem("t_copied")
        t_turned = sem("t_turned")
        moments_added = sem("moments_added")
        moments_copied = sem("moments_copied")
        moments_folded = sem("moments_folded")
        stage_step = sem("stage_step")
        scores_ready = sem("scores_ready")
        exp_done = sem("exp_done")
        attn_ready = sem("attn_ready")
        v_done = sem("v_done")
        v_high_ready = sem("v_high_ready")
        v_ready = sem("v_ready")
        y_done = sem("y_done")
        high_ready = sem("high_ready")
        low_ready = sem("low_ready")
        wy_done = sem("wy_done")
        wy_copied = sem("wy_copied")
        early_out_ready = sem("early_out_ready")
        dve_out_ready = sem("dve_out_ready")
        pool_out_ready = sem("pool_out_ready")
        DVE_STEPS = 4

        block = ctx.enter_context(nc.Block())

        @block.sync
        def _(sp):
            def load(image, p):
                loaded = x_loaded_early if is_early(image, p) else x_loaded
                sp.dma_start(x_of(image, p), x_blocks[image, :, :, bass.ts(p, PAIR)]).then_inc(loaded[p], 16)

            def store(image, p):
                sp.dma_start(out_blocks[image, :, :, bass.ts(p, PAIR)], stage[:, p % STAGES])\
                  .then_inc(stored[p % STAGES], 16)

            def traffic(image):
                stores = 0
                for p in range(PAIRS):
                    if is_early(image, p):
                        sp.wait_ge(early_out_ready, early_outputs(p, LAST))
                    else:
                        pairs = outputs(image, p) if is_first(image) else sp.snap(outputs(image, p))
                        sp.wait_ge(dve_out_ready, pairs)
                        sp.wait_ge(pool_out_ready, pairs)
                        load(image + 1, p)
                    while stores <= stores_after(image, p):
                        store(image, stores)
                        stores += 1

            sp.dma_start(weights_sb[:], weights).then_inc(weights_loaded, 16)
            sp.dma_start(w_sb[:], w_wT).then_inc(weights_loaded, 16)
            for p in range(PAIRS):
                load(0, p)
            for p in range(STAGES):
                load(1, p)
            traffic(0)
            with sp.Fori(1, IMAGES - 1) as image:
                traffic(image)
            for p in range(PAIRS):
                sp.wait_ge(dve_out_ready, outputs(IMAGES - 1, p))
                sp.wait_ge(pool_out_ready, outputs(IMAGES - 1, p))
                store(IMAGES - 1, p)
            for n in range(STAGES):
                sp.wait_ge(stored[n], 16 * TURNS * IMAGES)

        @block.gpsimd
        def _(pool):
            pool.memset(ident[:], 0.0).then_inc(zeroed, 1)
            pool.wait_ge(zeroed, 1)
            pool.affine_select(out=ident[:], in_=ident[:], compare_op=ALU.not_equal, fill=1.0, base=0,
                               pattern=[[-1, P]], channel_multiplier=1).then_inc(ident_ready, 1)

            def add_x(image):
                for p in range(STAGES if is_first(image) else 0, PAIRS):
                    block_out = stage[:, p % STAGES, LAST, :]
                    pool.wait_ge(wy_copied, outputs(image, p))
                    pool.tensor_tensor(block_out, block_out, x_sb[:, p, LAST, :], ALU.add)\
                        .then_inc(pool_out_ready, 1)

            add_x(0)
            with pool.Fori(1, IMAGES) as image:
                add_x(image)

        @block.tensor
        def _(pe):
            def theta(image, n):
                for p in range(TILE_PAIRS * n, TILE_PAIRS * (n + 1)):
                    if is_early(image, p):
                        pe.wait_ge(x_loaded_early[p], 16)
                    elif p < STAGES:
                        pe.wait_ge(x_loaded[p], image * 16)
                    else:
                        pe.wait_ge(x_loaded[p], (image + 1) * 16)
                if not (n == 0 and is_first(image)):
                    pe.wait_ge(t_copied, image * TILES + n)
                for k in range(KB):
                    for q in range(QUADS):
                        mm = pe.matmul(ps_t[q * IC:(q + 1) * IC, :], theta_sb[:, k, :],
                                       x_of(image, TILE_PAIRS * n + q // 2)[:, k, bass.ts(q % 2, CHUNK)],
                                       start=(k == 0), stop=(k == KB - 1))
                mm.then_inc(theta_done, 1)

            def moments_of(image, n):
                pe.wait_ge(t_turned, image * TILES + (n + 1))
                for a in range(GROUPS):
                    mm = pe.matmul(ps_moments, tT[:, a, 0:P], tT[:, a, 0:P + 1],
                                   start=(n == 0 and a == 0), stop=(n == TILES - 1 and a == GROUPS - 1))
                mm.then_inc(moments_added, 1)

            def project(image, p):
                for k in range(KB):
                    for c in range(2):
                        mm = pe.matmul(ps_y[2 * c * IC:2 * (c + 1) * IC, p % 2, :], g_sb[:, k, :],
                                       x_of(image, p)[:, k, bass.ts(c, CHUNK)], start=(k == 0), stop=(k == KB - 1))
                mm.then_inc(y_done, 1)

            def expand(image, p):
                pe.wait_ge(low_ready, image * (2 * PAIRS) + 2 * (p + 1))
                if p == 0:
                    pe.wait_ge(v_ready, image + 1)
                for k in range(KB):
                    if p > 0 and is_early(image, p - 1):
                        pe.wait_ge(early_out_ready, early_outputs(p - 1, k))
                    elif p > 0:
                        pe.wait_ge(wy_copied if k == LAST else dve_out_ready, outputs(image, p - 1))
                    for c in range(2):
                        mm = pe.matmul(ps_out[:, k, bass.ts(c, CHUNK)], v_split[:, bass.ts(k, P)],
                                       y_split[:, p % 2, c, :], start=True, stop=True)
                    mm.then_inc(wy_done, 1)

            def attention(image):
                pe.wait_ge(moments_copied, image + 1)
                for q in range(QUADS):
                    pe.matmul(ps_second, ident[:, bass.ts(q, IC)], moments[:, bass.ts(q, IC)],
                              start=(q == 0), stop=(q == QUADS - 1))
                pe.matmul(ps_row, moments[:, P:P + 1].to_broadcast([P, IC]), fold[:], start=True, stop=True)
                pe.matmul(ps_col, fold[:], moments[:, P:P + 1], start=True, stop=True).then_inc(moments_folded, 1)
                project(image, 0)
                pe.wait_ge(attn_ready, image + 1)
                pe.matmul(ps_v, attn4, w_sb[:], start=True, stop=True).then_inc(v_done, 1)
                project(image, 1)

            def phase2(image, p, beside=None):
                expand(image, p)
                if beside is not None:
                    beside()
                if p + 2 < PAIRS:
                    project(image, p + 2)

            def both_phases(image):
                for j in range(TILES):
                    n = phase1_tile(j)
                    phase1 = [None, None] if n is None else [lambda: theta(image + 1, n), lambda: moments_of(image + 1, n)]
                    for p, beside in zip(range(TILE_PAIRS * j, TILE_PAIRS * (j + 1)), phase1):
                        phase2(image, p, beside)
                for n in range(TILES - PHASE1_LAG, TILES):
                    theta(image + 1, n)
                    moments_of(image + 1, n)
                attention(image + 1)

            pe.wait_ge(weights_loaded, 2 * 16)
            pe.wait_ge(constants_ready, 2)
            for n in range(TILES):
                theta(0, n)
                moments_of(0, n)
            attention(0)
            both_phases(0)
            with pe.Fori(1, IMAGES - 1) as image:
                both_phases(image)
            for p in range(PAIRS):
                phase2(IMAGES - 1, p)

        @block.scalar
        def _(act):
            def copy_t(image, n):
                act.wait_ge(theta_done, image * TILES + (n + 1))
                if not (n == 0 and is_first(image)):
                    act.wait_ge(t_turned, image * TILES + n)
                act.activation(t_sb[:], ps_t[:], ACT.Identity, bias=theta_bias[:]).then_inc(t_copied, 1)

            def split_high(image, p):
                act.wait_ge(y_done, image * PAIRS + (p + 1))
                if p >= 2:
                    act.wait_ge(wy_done, image * (PAIRS * KB) + (p - 1) * KB)
                for c in range(2):
                    rows = slice(2 * c * IC, 2 * (c + 1) * IC)
                    act.activation(y_split[rows, p % 2, c, :], ps_y[rows, p % 2, :], ACT.Identity,
                                   bias=g_bias[rows, :]).then_inc(high_ready, 1)

            def copy_wy(image, p):
                act.wait_ge(stored[p % STAGES], image * (16 * TURNS) + 16 * (p // STAGES))
                act.wait_ge(wy_done, image * (PAIRS * KB) + (p + 1) * KB)
                act.activation(stage[:, p % STAGES, LAST, :], ps_out[:, LAST, :], ACT.Identity,
                               bias=w_bias[:, LAST:KB]).then_inc(wy_copied, 1)

            def attention(image):
                act.wait_ge(moments_added, image * TILES + TILES)
                act.activation(moments, ps_moments, ACT.Copy).then_inc(moments_copied, 1)
                act.wait_ge(scores_ready, image + 1)
                act.activation(exps, cov, ACT.Exp, bias=neg_max, scale=SOFTMAX_SCALE,
                               accum_out=row_sum).then_inc(exp_done, 1)
                split_high(image, 0)
                act.wait_ge(v_done, image + 1)
                act.activation(v_split[:], ps_v, ACT.Copy).then_inc(v_high_ready, 1)

            def phase2(image, p):
                if p + 1 < PAIRS:
                    split_high(image, p + 1)
                if not is_early(image, p):
                    copy_wy(image, p)

            def both_phases(image):
                for j in range(TILES):
                    n = phase1_tile(j)
                    for p in range(TILE_PAIRS * j, TILE_PAIRS * (j + 1)):
                        phase2(image, p)
                        if n is not None and p == TILE_PAIRS * j:
                            copy_t(image + 1, n)
                for n in range(TILES - PHASE1_LAG, TILES):
                    copy_t(image + 1, n)
                attention(image + 1)

            act.wait_ge(weights_loaded, 2 * 16)
            for n in range(TILES):
                copy_t(0, n)
            attention(0)
            both_phases(0)
            with act.Fori(1, IMAGES - 1) as image:
                both_phases(image)
            for p in range(PAIRS):
                phase2(IMAGES - 1, p)

        @block.vector
        def _(dve):
            def turn_t(image, n):
                dve.wait_ge(t_copied, image * TILES + (n + 1))
                if not (n == 0 and is_first(image)):
                    dve.wait_ge(moments_added, image * TILES + n)
                dve.transpose(tT[:, :, 0:P], t_sb[:].rearrange("p (a c) -> p a c", c=P)).then_inc(t_turned, 1)

            def split_low(image, p):
                for c in range(2):
                    rows = slice(2 * c * IC, 2 * (c + 1) * IC)
                    others = slice(2 * (1 - c) * IC, 2 * (2 - c) * IC)
                    dve.wait_ge(high_ready, image * (2 * PAIRS) + (2 * p + c + 1))
                    dve.scalar_tensor_tensor(out=y_split[others, p % 2, c, :], in0=ps_y[rows, p % 2, :],
                                             scalar=g_bias[rows, :], in1=y_split[rows, p % 2, c, :].bitcast(fp32),
                                             op0=ALU.add, op1=ALU.subtract).then_inc(low_ready, 1)

            def add_out(image, p):
                if not is_early(image, p):
                    dve.wait_ge(stored[p % STAGES], image * (16 * TURNS) + 16 * (p // STAGES))
                for k in range(KB if is_early(image, p) else LAST):
                    dve.wait_ge(wy_done, image * (PAIRS * KB) + (p * KB + k + 1))
                    dve.scalar_tensor_tensor(out=stage[:, p % STAGES, k, :], in0=ps_out[:, k, :],
                                             scalar=w_bias[:, k:k + 1], in1=x_of(image, p)[:, k, :],
                                             op0=ALU.add, op1=ALU.add)\
                       .then_inc(early_out_ready if is_early(image, p) else dve_out_ready, 1)

            def attention(image):
                steps = [0]

                def step(instruction):
                    steps[0] += 1
                    instruction.then_inc(stage_step, 1)
                    dve.wait_ge(stage_step, image * DVE_STEPS + steps[0])

                dve.wait_ge(moments_folded, image + 1)
                step(dve.tensor_scalar(neg_mean_row, ps_row, -1.0 / M, None, ALU.mult))
                step(dve.scalar_tensor_tensor(out=cov, in0=neg_mean_row, scalar=ps_col, in1=ps_second,
                                              op0=ALU.mult, op1=ALU.add))
                step(dve.tensor_reduce(row_max, cov, AX.X, ALU.max))
                dve.tensor_scalar(neg_max, row_max, -SOFTMAX_SCALE, None, ALU.mult).then_inc(scores_ready, 1)
                dve.wait_ge(exp_done, image + 1)
                step(dve.reciprocal(row_recip, row_sum))
                dve.tensor_scalar(attn4.rearrange("p (q c) -> p q c", q=QUADS),
                                  exps.unsqueeze(1).to_broadcast([IC, QUADS, IC]), row_recip, None,
                                  ALU.mult).then_inc(attn_ready, 1)
                split_low(image, 0)
                dve.wait_ge(v_high_ready, image + 1)
                for q in range(1, QUADS, 2):
                    rows = slice(q * IC, (q + 1) * IC)
                    low = dve.tensor_tensor(v_split[rows, :], ps_v[rows, :], v_split[rows, :].bitcast(fp32),
                                            ALU.subtract)
                low.then_inc(v_ready, 1)
                assert steps[0] == DVE_STEPS

            def phase2(image, p):
                if p + 1 < PAIRS:
                    split_low(image, p + 1)
                add_out(image, p)

            def both_phases(image):
                for j in range(TILES):
                    n = phase1_tile(j)
                    for p in range(TILE_PAIRS * j, TILE_PAIRS * (j + 1)):
                        phase2(image, p)
                        if n is not None and p == TILE_PAIRS * j:
                            turn_t(image + 1, n)
                for n in range(TILES - PHASE1_LAG, TILES):
                    turn_t(image + 1, n)
                attention(image + 1)

            dve.memset(tT[:], 1.0).then_inc(constants_ready, 1)
            dve.wait_ge(ident_ready, 1)
            dve.tensor_reduce(fold[:], ident[:].rearrange("p (q c) -> p c q", q=QUADS), AX.X, ALU.add)\
               .then_inc(constants_ready, 1)
            dve.wait_ge(constants_ready, 2)
            dve.wait_ge(weights_loaded, 2 * 16)
            for n in range(TILES):
                turn_t(0, n)
            attention(0)
            both_phases(0)
            with dve.Fori(1, IMAGES - 1) as image:
                both_phases(image)
            for p in range(PAIRS):
                phase2(IMAGES - 1, p)


def kernel(x, L0_conv_g_w, L0_conv_g_b, L0_conv_theta_w, L0_conv_theta_b, L0_conv_w_w, L0_conv_w_b):
    import numpy as _np
    import concourse.bacc as _bacc
    from concourse import mybir as _mybir
    from concourse.bass_utils import run_bass_kernel_spmd as _run

    B, C, H, W = x.shape
    P = 128
    theta_w, g_w, w_w = (_np.asarray(a) for a in (L0_conv_theta_w, L0_conv_g_w, L0_conv_w_w))
    IC = theta_w.shape[0]

    def by_blocks(a):
        return a.reshape(a.shape[0], C // P, P).transpose(2, 1, 0)

    weights = _np.concatenate(
        [
            by_blocks(theta_w).reshape(P, -1),
            by_blocks(_np.concatenate([g_w, g_w])).reshape(P, -1),
            _np.tile(_np.asarray(L0_conv_theta_b), P // IC).reshape(P, 1),
            _np.tile(_np.asarray(L0_conv_g_b), P // IC).reshape(P, 1),
            _np.asarray(L0_conv_w_b).reshape(C // P, P).T,
        ],
        axis=1,
    )
    given = {
        "x": _np.asarray(x).reshape(B, C, H * W),
        "weights": _np.ascontiguousarray(weights),
        "w_wT": _np.ascontiguousarray(w_w.T),
    }
    nc = _bacc.Bacc("TRN2", target_bir_lowering=False, num_devices=1)
    arrays, args = {}, []
    for name, a in given.items():
        arrays[f"in_{name}_dram"] = a
        args.append(nc.dram_tensor(f"in_{name}_dram", a.shape, _mybir.dt.from_np(a.dtype), kind="ExternalInput").ap())
    args.append(nc.dram_tensor("out_dram", (B, C, H * W), _mybir.dt.float32, kind="ExternalOutput").ap())
    covariance_attention_kernel(nc, *args)
    r = _run(nc, [arrays], core_ids=[0])
    return r.results[0]["out_dram"].reshape(B, C, H, W)
```
